# Optimizing a Trainium2 kernel written in Bass

```python
import numpy as np
import jax
import jax.numpy as jnp

def _softmax(x, axis=-1):
    return jax.nn.softmax(x, axis=axis)

def _gelu(x):
    return jax.nn.gelu(x, approximate=True)

def _silu(x):
    return jax.nn.silu(x)

def _sigmoid(x):
    return jax.nn.sigmoid(x)

def _layernorm(x, axis=-1, eps=1e-05):
    m = jnp.mean(x, axis=axis, keepdims=True)
    v = jnp.var(x, axis=axis, keepdims=True)
    return (x - m) / jnp.sqrt(v + eps)

def _scatter_add(tgt, idx, src, axis=0):
    return tgt.at[idx].add(src)

def _segment_sum(src, seg, n):
    return jax.ops.segment_sum(src, seg, n)
kernel_name = 'mk_cond_resid_d2_seqx_r2_223f79'

def setup_inputs(seed: int=0):
    np.random.seed(seed)
    _w = jnp.asarray

    def _rec_inputs():
        import jax
        import jax.numpy as jnp
        _rk = jax.random.key(seed)
        x = -0.0003929 + 0.9999 * jax.random.normal(jax.random.fold_in(_rk, 1), (2, 2048, 512), jnp.float32)
        _lenS = 2048 - jax.random.randint(jax.random.fold_in(_rk, 7), (2,), 0, max(1, 2048 // 4) + 1, jnp.int32)
        _lenS2 = 2048 - jax.random.randint(jax.random.fold_in(_rk, 8), (2,), 0, max(1, 2048 // 4) + 1, jnp.int32)
        itok_B_0_2 = jax.random.randint(jax.random.fold_in(_rk, 11), (2,), 0, 3, jnp.int32)
        itok_B_0_63 = jax.random.randint(jax.random.fold_in(_rk, 12), (2,), 0, 64, jnp.int32)
        return (x, itok_B_0_2, itok_B_0_63)
    x, itok_B_0_2, itok_B_0_63 = _rec_inputs()

    def _L0_cond_setup():
        import jax, jax.numpy as jnp
        import numpy as np
        B, S, D, F, E = (8, 1024, 512, 2048, 5)

        def _dense(x, wi_, wo_):
            return jax.nn.relu(x @ wi_) @ wo_
        key = jax.random.key(seed)
        ks = jax.random.split(key, 9)
        sc = 0.02
        return {'hidden_states': jax.random.normal(ks[0], (B, S, D), jnp.float32), 'type_label': jax.random.randint(ks[1], (B,), 0, E, jnp.int32), 'wi': jax.random.normal(ks[2], (E, D, F), jnp.float32) * sc, 'wo': jax.random.normal(ks[3], (E, F, D), jnp.float32) * sc, 'swi': jax.random.normal(ks[4], (2, D, F), jnp.float32) * sc, 'swo': jax.random.normal(ks[5], (2, F, D), jnp.float32) * sc, 'g1': jax.random.normal(ks[6], (3 * D, D), jnp.float32) * sc, 'g2': jax.random.normal(ks[7], (D, 3), jnp.float32) * sc}
    _L0_cond_all = _L0_cond_setup()
    _L0_cond_in = {k: v for k, v in _L0_cond_all.items() if k in ('wi', 'wo', 'swi', 'swo', 'g1', 'g2')}
    del _L0_cond_all

    def _L1_cond_setup():
        import jax, jax.numpy as jnp
        import numpy as np
        NUM_CATEGORIES = 64
        INPUT_DIM = 512
        HIDDEN_DIM = 512
        B = 128
        S = 64
        key = jax.random.key(seed)
        kx, kc, kw = jax.random.split(key, 3)
        x = jax.random.normal(kx, (B, S, INPUT_DIM), dtype=jnp.float32)
        cat_ids = jax.random.randint(kc, (B,), 0, NUM_CATEGORIES, dtype=jnp.int32)
        W = 0.02 * jax.random.normal(kw, (NUM_CATEGORIES, INPUT_DIM, HIDDEN_DIM), dtype=jnp.float32)
        b = jnp.zeros((NUM_CATEGORIES, HIDDEN_DIM), dtype=jnp.float32)
        return {'x': x, 'cat_ids': cat_ids, 'W': W, 'b': b}
    _L1_cond_all = _L1_cond_setup()
    _L1_cond_in = {k: v for k, v in _L1_cond_all.items() if k in ('W', 'b')}
    del _L1_cond_all
    return {'x': x, 'itok_B_0_2': itok_B_0_2, 'itok_B_0_63': itok_B_0_63, 'L0_cond_wi': _L0_cond_in['wi'], 'L0_cond_wo': _L0_cond_in['wo'], 'L0_cond_swi': _L0_cond_in['swi'], 'L0_cond_swo': _L0_cond_in['swo'], 'L0_cond_g1': _L0_cond_in['g1'], 'L0_cond_g2': _L0_cond_in['g2'], 'L1_cond_W': _L1_cond_in['W'], 'L1_cond_b': _L1_cond_in['b']}

def reference(x, itok_B_0_2, itok_B_0_63, L0_cond_wi, L0_cond_wo, L0_cond_swi, L0_cond_swo, L0_cond_g1, L0_cond_g2, L1_cond_W, L1_cond_b):
    import jax
    import jax.numpy as jnp

    def _L0_cond_ref(hidden_states, type_label, wi, wo, swi, swo, g1, g2):
        import jax, jax.numpy as jnp
        import numpy as np
        B, S, D, F, E = (8, 1024, 512, 2048, 5)

        def _dense(x, wi_, wo_):
            return jax.nn.relu(x @ wi_) @ wo_
        x = hidden_states
        s0 = _dense(x, swi[0], swo[0])
        s1 = _dense(x, swi[1], swo[1])
        wi_sel = wi[type_label]
        wo_sel = wo[type_label]
        h = jax.nn.relu(jnp.einsum('bsd,bdf->bsf', x, wi_sel))
        eo = jnp.einsum('bsf,bfd->bsd', h, wo_sel)
        gate_in = jnp.concatenate([eo[:, 0], s0[:, 0], s1[:, 0]], axis=-1)
        w = jax.nn.softmax(jax.nn.relu(gate_in @ g1) @ g2, axis=-1)
        w = w[:, :, None, None]
        return eo * w[:, 0] + s0 * w[:, 1] + s1 * w[:, 2]

    def _L1_cond_ref(x, cat_ids, W, b):
        import jax, jax.numpy as jnp
        import numpy as np
        NUM_CATEGORIES = 64
        INPUT_DIM = 512
        HIDDEN_DIM = 512
        B = 128
        S = 64
        selected_W = W[cat_ids]
        selected_b = b[cat_ids]
        out = jnp.einsum('bsd,bdh->bsh', x, selected_W) + selected_b[:, None, :]
        return out
    x = x + _L0_cond_ref(x, itok_B_0_2, L0_cond_wi, L0_cond_wo, L0_cond_swi, L0_cond_swo, L0_cond_g1, L0_cond_g2)
    x = x + _L1_cond_ref(x, itok_B_0_63, L1_cond_W, L1_cond_b)
    return x

_drawn_inputs = setup_inputs


def setup_inputs(seed=0):
    import zlib

    import numpy as np

    out = dict(_drawn_inputs(seed))
    spreads = {'L1_cond_b': (0.0, 0.1)}
    factors = {'L0_cond_g1': 8.0, 'L0_cond_g2': 8.0}
    for name, (base, spread) in spreads.items():
        noise = np.random.default_rng([zlib.crc32(name.encode()), seed]).standard_normal(out[name].shape)
        drawn = base * np.exp(spread * noise) if base else spread * noise
        out[name] = jnp.asarray(drawn.astype(out[name].dtype))
    for name, factor in factors.items():
        out[name] = (out[name] * factor).astype(out[name].dtype)
    return out
```

```python
from contextlib import ExitStack

import concourse.bass as bass
from concourse import mybir

F32 = mybir.dt.float32
F32R = mybir.dt.float32r
I32 = mybir.dt.int32
ALU = mybir.AluOpType
ACT = mybir.ActivationFunctionType
AX_X = mybir.AxisListType.X

P = 128
D = 512
F = 2048
KD = D // P
TB = 512
TT = TB // P
NBATCH, SEQ = 2, 2048
SUPERS = NBATCH * SEQ // (2 * TB)
NETS = 3
GF = 256
GC = GF // P
GROUPS = NETS * F // GF
PAIRS = GROUPS // 2
NET_PAIRS = PAIRS // NETS
WCOLS = KD * GF + GC * D
PIECE = 512
PIECES = WCOLS // PIECE
UNITS = 8
GATE_PART = [1, 2, 0]


def build(nc, x, expert_id, category_id, wi, wo, swi, swo, g1, g2, W, bias, out):
    x_blk = x.rearrange("a (n p t) d -> (a n) p t d", p=P, t=TT)
    out_blk = out.rearrange("a (n p t) d -> (a n) p t d", p=P, t=TT)
    wi_v = wi.rearrange("e (k p) f -> e p k f", p=P)
    wo_v = wo.rearrange("e (c p) d -> e p c d", p=P)
    swi_v = swi.rearrange("e (k p) f -> e p k f", p=P)
    swo_v = swo.rearrange("e (c p) d -> e p c d", p=P)
    g1_v = g1.rearrange("(i k p) m -> i p k m", p=P, k=KD)
    g2_v = g2.rearrange("(k p) c -> p k c", p=P)
    W_v = W.rearrange("e (k p) h -> e p k h", p=P)

    ctx = ExitStack()
    with ctx:
        def sb(name, shape, dt=F32):
            return ctx.enter_context(nc.sbuf_tensor(name, shape, dt))

        def sem(name):
            return ctx.enter_context(nc.semaphore(name))

        xh = sb("xh", [P, 2, 2, KD, TB], F32R)
        xl = sb("xl", [P, 2, 2, KD, TB], F32R)
        Y = sb("Y", [P, NETS, 2, KD, TB])
        wh = sb("wh", [P, 2, WCOLS], F32R)
        wl = sb("wl", [P, 2, WCOLS], F32R)
        wraw = sb("wraw", [P, 2, WCOLS])
        hh = sb("hh", [P, 2, TB], F32R)
        hl = sb("hl", [P, 2, TB], F32R)
        Wh = sb("Wh", [P, KD, D], F32R)
        Wl = sb("Wl", [P, KD, D], F32R)
        xaux = sb("xaux", [P, KD, TB])
        gaux = sb("gaux", [P, KD, D])
        gacc = sb("gacc", [P, D])
        bias_bc = sb("bias_bc", [P, D])
        ident = sb("ident", [P, P])
        ones = sb("ones", [P, P])
        g2s = sb("g2s", [P, KD, NETS])
        gt = sb("gt", [P, KD])
        gp = sb("gp", [P, KD, NETS])
        nmax = sb("nmax", [P, 1])
        gexp = sb("gexp", [P, NETS])
        gsum = sb("gsum", [P, 1])
        ginv = sb("ginv", [P, 1])
        gw = sb("gw", [P, NETS])
        ids = sb("ids", [1, 4], I32)

        yps = [ctx.enter_context(nc.psum_tensor(f"yps{j}", [P, TB], F32)) for j in range(KD)]
        hps = [ctx.enter_context(nc.psum_tensor(f"hps{j}", [P, TB], F32)) for j in range(2)]
        aps = [ctx.enter_context(nc.psum_tensor(f"aps{j}", [P, TB], F32)) for j in range(2)]

        s_ids = sem("ids_loaded")
        s_x = [sem("x_loaded_even"), sem("x_loaded_odd")]
        s_w = [sem("weights_loaded_0"), sem("weights_loaded_1")]
        s_g = sem("gaux_loaded")
        s_g2 = sem("g2_loaded")
        s_bias = sem("bias_loaded")
        s_stored = [sem("out_stored_block_0"), sem("out_stored_block_1")]
        s_c = sem("constants_set")
        s_ident = sem("ident_cleared")
        s_xtr = sem("x_transposed")
        s_xhi = sem("x_high_split")
        s_xlo = sem("x_low_split")
        s_whi = sem("weights_high_split")
        s_wrdy = sem("weights_ready")
        s_hps = sem("hidden_in_psum")
        s_hhi = sem("hidden_high_split")
        s_hrdy = sem("hidden_ready")
        s_yps = sem("net_out_in_psum")
        s_yacc = sem("net_out_accumulated")
        s_zero = sem("net_out_cleared")
        s_gused = sem("gaux_used")
        s_gch = sem("gate_vector_step")
        s_gps = sem("gate_product_in_psum")
        s_grelu = sem("gate_hidden_ready")
        s_gexp = sem("gate_exp_ready")
        s_gmix = sem("gate_product_ready")
        s_gmax = sem("gate_max_ready")
        s_xs = sem("x_summed")
        s_mix = sem("mix_step")
        s_chi = sem("x2_high_split")
        s_clo = sem("x2_low_split")
        s_Wi = sem("category_identity_added")
        s_Whi = sem("category_high_split")
        s_Wrdy = sem("category_ready")
        s_ops = sem("out_in_psum")
        s_oev = sem("out_evacuated")

        block = ctx.enter_context(nc.Block())

        @block.sync
        def _(sp):
            def load_weights(s, net, p, j, e):
                m = s * GROUPS + net * 2 * NET_PAIRS + 2 * p + j
                f0 = p * 2 * GF + j * GF
                c0 = p * 2 * GC + j * GC
                if not isinstance(m, int) or m >= 2:
                    sp.wait_ge(s_wrdy, m - 1)
                src_i, src_o, n = (swi_v, swo_v, net) if net < 2 else (wi_v, wo_v, e)
                sp.dma_start(wraw[:, j, 0:KD * GF].rearrange("p (k f) -> p k f", k=KD),
                             src_i[n, :, :, bass.ds(f0, GF)]).then_inc(s_w[j], 16)
                sp.dma_start(wraw[:, j, KD * GF:WCOLS].rearrange("p (c d) -> p c d", c=GC),
                             src_o[n, :, bass.ds(c0, GC), :]).then_inc(s_w[j], 16)

            sp.dma_start(xaux[:, :, :], x_blk[0, :, :, :]).then_inc(s_x[0], 16)
            load_weights(0, 0, 0, 0, None)
            sp.dma_start(gaux[:, :, :], x_blk[1, :, :, :]).then_inc(s_x[1], 16)
            load_weights(0, 0, 0, 1, None)
            sp.dma_start(ids[:, 0:2], expert_id.rearrange("(a n) -> a n", a=1)).then_inc(s_ids, 16)
            sp.dma_start(ids[:, 2:4], category_id.rearrange("(a n) -> a n", a=1)).then_inc(s_ids, 16)
            sp.dma_start(g2s[:, :, :], g2_v).then_inc(s_g2, 16)
            sp.wait_ge(s_ids, 32)
            experts = [sp.value_load(ids[0:1, b:b + 1], min_val=0, max_val=wi.shape[0] - 1) for b in range(NBATCH)]
            cats = [sp.value_load(ids[0:1, 2 + b:3 + b], min_val=0, max_val=W.shape[0] - 1) for b in range(NBATCH)]

            def store(t):
                sp.wait_ge(s_oev, TT * (t + 1))
                sp.dma_start(out_blk[t, :, :, :], Y[:, 1, t % 2, :, :]).then_inc(s_stored[t % 2], 16)

            for s in range(SUPERS):
                b, first_half = s // 2, s % 2 == 0
                e = experts[b]
                if s > 0:
                    load_weights(s, 0, 0, 0, e)
                    load_weights(s, 0, 0, 1, e)
                    sp.wait_ge(s_xtr, 8 * s + 4)
                    sp.dma_start(xaux[:, :, :], x_blk[2 * s + 1, :, :, :]).then_inc(s_x[1], 16)
                if first_half:
                    if s == 0:
                        sp.wait_ge(s_xtr, 8)
                    else:
                        sp.wait_ge(s_gused, 4 * b)
                    sp.dma_start(gaux[:, :, :], g1_v[GATE_PART[0], :, :, :]).then_inc(s_g, 16)
                load_weights(s, 0, 1, 0, e)
                load_weights(s, 0, 1, 1, e)
                load_weights(s, 0, 2, 0, e)
                if s > 0:
                    store(2 * s - 2)
                    store(2 * s - 1)
                if first_half:
                    sp.dma_start(bias_bc[:, :], bias[bass.ds(cats[b], 1), :].to_broadcast([P, D])).then_inc(s_bias, 16)
                load_weights(s, 0, 2, 1, e)
                load_weights(s, 0, 3, 0, e)
                load_weights(s, 0, 3, 1, e)
                with sp.Fori(0, 2) as p:
                    for j in range(2):
                        load_weights(s, 1, p, j, e)
                if first_half:
                    sp.wait_ge(s_gused, 4 * b + 1)
                    sp.dma_start(gaux[:, :, :], W_v[cats[b], :, :, :]).then_inc(s_g, 16)
                if s + 1 < SUPERS:
                    if s > 0:
                        sp.wait_ge(s_mix, 12 * (2 * s - 1) + 4)
                    else:
                        sp.wait_ge(s_xtr, 4)
                    sp.dma_start(xaux[:, :, :], x_blk[2 * s + 2, :, :, :]).then_inc(s_x[0], 16)
                with sp.Fori(2, 4) as p:
                    for j in range(2):
                        load_weights(s, 1, p, j, e)
                if first_half:
                    sp.wait_ge(s_gused, 4 * b + 2)
                    sp.dma_start(gaux[:, :, :], g1_v[GATE_PART[1], :, :, :]).then_inc(s_g, 16)
                with sp.Fori(0, 2) as p:
                    for j in range(2):
                        load_weights(s, 2, p, j, e)
                if first_half:
                    sp.wait_ge(s_gused, 4 * b + 3)
                    sp.dma_start(gaux[:, :, :], g1_v[GATE_PART[2], :, :, :]).then_inc(s_g, 16)
                with sp.Fori(2, 4) as p:
                    for j in range(2):
                        load_weights(s, 2, p, j, e)
            store(2 * SUPERS - 2)
            store(2 * SUPERS - 1)
            for k in range(2):
                sp.wait_ge(s_stored[k], 16 * SUPERS)

        @block.gpsimd
        def _(pool):
            pool.memset(ident[:, :], 0.0).then_inc(s_ident, 1)
            pool.wait_ge(s_ident, 1)
            pool.affine_select(out=ident[:, :], in_=ident[:, :], compare_op=ALU.not_equal, fill=1.0,
                               base=0, pattern=[[-1, P]], channel_multiplier=1).then_inc(s_c, 1)
            pool.memset(ones[:, :], 1.0).then_inc(s_c, 1)
            pool.memset(Y[:, 1, :, :, :], 0.0).then_inc(s_zero, 1)
            pool.memset(Y[:, 2, :, :, :], 0.0).then_inc(s_zero, 1)
            for s in range(SUPERS):
                q = s % 2
                for k in range(2):
                    if k == 0:
                        pool.wait_ge(s_xtr, 8 * min(s + 2, SUPERS))
                        pool.wait_ge(s_xlo, 8 * (s + 1))
                        if s > 0:
                            pool.wait_ge(s_mix, 12 * (2 * s - 1) + 4)
                    else:
                        pool.wait_ge(s_mix, 12 * 2 * s + 4)
                    pool.tensor_tensor(xaux[:, :, :], xh[:, q, k, :, :].bitcast(F32),
                                       xl[:, q, k, :, :].bitcast(F32), ALU.add).then_inc(s_xs, 1)
                if s + 1 < SUPERS:
                    for k in range(2):
                        pool.wait_ge(s_clo, KD * (2 * s + k + 1))
                        pool.memset(Y[:, 2, k, :, :], 0.0).then_inc(s_zero, 1)
                    for k in range(2):
                        pool.wait_ge(s_stored[k], 16 * (s + 1))
                        pool.memset(Y[:, 1, k, :, :], 0.0).then_inc(s_zero, 1)

        @block.scalar
        def _(act):
            def hidden_high(U, i):
                act.wait_ge(s_hps, U + 1)
                act.activation(hh[:, i % 2, :], hps[i % 2][:, :], ACT.Relu).then_inc(s_hhi, 1)

            def split_high(pair, slot, m):
                act.wait_ge(s_w[slot], 32 * (pair + 1))
                for c in range(PIECES):
                    cols = slice(c * PIECE, (c + 1) * PIECE)
                    act.activation(wh[:, slot, cols], wraw[:, slot, cols], ACT.Copy).then_inc(s_whi, 1)

            def x_high(s, k):
                for d in range(KD):
                    X = 8 * s + 4 * k + d
                    act.wait_ge(s_xtr, X + 1)
                    act.activation(xh[:, s % 2, k, d, :], aps[X % 2][:, :], ACT.Copy).then_inc(s_xhi, 1)

            def x2_high(s, k):
                for d in range(KD):
                    act.wait_ge(s_mix, 12 * (2 * s + k) + 8 + d + 1)
                    act.activation(xh[:, s % 2, k, d, :], Y[:, 2, k, d, :], ACT.Copy).then_inc(s_chi, 1)

            def steps(s, p, which):
                pair = s * PAIRS + p
                for v in range(UNITS):
                    end = which == "last" and v == UNITS - 1 and s == SUPERS - 1
                    if not end:
                        hidden_high(UNITS * pair + v + 1, v + 1)
                    if v == 0:
                        split_high(pair, 1, 2 * pair + 1)
                    if v == 4 and not (which == "last" and s == SUPERS - 1):
                        split_high(pair + 1, 0, 2 * pair + 2)
                    if which == "first" and s > 0:
                        if v == 1:
                            x2_high(s - 1, 0)
                        if v == 2:
                            x2_high(s - 1, 1)
                    if which == "last":
                        if v == 2 and s + 1 < SUPERS:
                            x_high(s + 1, 0)
                        if v == 6:
                            if s + 1 < SUPERS:
                                x_high(s + 1, 1)
                            if s % 2 == 0:
                                act.wait_ge(s_gps, s + 1)
                                act.activation(gt[:, :], aps[0][:, 0:KD], ACT.Relu).then_inc(s_grelu, 1)
                        if v == 7 and s % 2 == 0:
                            act.wait_ge(s_gmax, s // 2 + 1)
                            act.activation(gexp[:, :], aps[1][:, 0:NETS], ACT.Exp, bias=nmax[:, 0:1],
                                           accum_out=gsum[:, 0:1]).then_inc(s_gexp, 1)

            x_high(0, 0)
            split_high(0, 0, 0)
            hidden_high(0, 0)
            x_high(0, 1)
            for s in range(SUPERS):
                steps(s, 0, "first")
                with act.Fori(1, 6) as p:
                    steps(s, p, "middle")
                if s % 2 == 0:
                    for d in range(KD):
                        act.wait_ge(s_Wi, 4 * (s // 2) + d + 1)
                        act.activation(Wh[:, d, :], gaux[:, d, :], ACT.Copy).then_inc(s_Whi, 1)
                with act.Fori(6, PAIRS - 1) as p:
                    steps(s, p, "middle")
                steps(s, PAIRS - 1, "last")
            for k in range(2):
                x2_high(SUPERS - 1, k)

        @block.vector
        def _(dve):
            def hidden_low(U, i):
                dve.wait_ge(s_hhi, U + 1)
                dve.scalar_tensor_tensor(out=hl[:, i % 2, :], in0=hps[i % 2][:, :], scalar=0.0,
                                         in1=hh[:, i % 2, :].bitcast(F32), op0=ALU.max,
                                         op1=ALU.subtract).then_inc(s_hrdy, 1)

            def split_low(slot, m):
                for c in range(PIECES):
                    cols = slice(c * PIECE, (c + 1) * PIECE)
                    dve.wait_ge(s_whi, PIECES * m + c + 1)
                    last = dve.tensor_tensor(wl[:, slot, cols], wraw[:, slot, cols],
                                             wh[:, slot, cols].bitcast(F32), ALU.subtract)
                last.then_inc(s_wrdy, 1)

            def accumulate(s, K, net, k, copy):
                for d in range(KD):
                    dve.wait_ge(s_yps, KD * K + d + 1)
                    if copy:
                        if s > 0:
                            dve.wait_ge(s_mix, 12 * (2 * s - 2 + k) + 8)
                        dve.tensor_copy(Y[:, net, k, d, :], yps[d][:, :]).then_inc(s_yacc, 1)
                    else:
                        dve.wait_ge(s_yacc, KD * K + d + 1 - 2 * KD)
                        dve.tensor_tensor(Y[:, net, k, d, :], yps[d][:, :], Y[:, net, k, d, :],
                                          ALU.add).then_inc(s_yacc, 1)

            def x_low(s, k):
                for d in range(KD):
                    X = 8 * s + 4 * k + d
                    dve.wait_ge(s_xhi, X + 1)
                    dve.tensor_tensor(xl[:, s % 2, k, d, :], aps[X % 2][:, :],
                                      xh[:, s % 2, k, d, :].bitcast(F32), ALU.subtract).then_inc(s_xlo, 1)

            chain = [0]

            def link(ins):
                chain[0] += 1
                ins.then_inc(s_gch, 1)
                dve.wait_ge(s_gch, chain[0])

            def gate_partial(b, net):
                n = [0, 2, 3][net]
                dve.wait_ge(s_g, 16 * (4 * b + n + 1))
                K = 4 * ((2 * b) * PAIRS + (net + 1) * NET_PAIRS) - 2
                dve.wait_ge(s_yacc, KD * (K + 1))
                for d in range(KD):
                    scalar = Y[:, net, 0, d, 0:1]
                    if net == 0 and d == 0:
                        link(dve.tensor_scalar(gacc[:, :], gaux[:, d, :], scalar, None, ALU.mult))
                    else:
                        link(dve.scalar_tensor_tensor(out=gacc[:, :], in0=gaux[:, d, :], scalar=scalar,
                                                      in1=gacc[:, :], op0=ALU.mult, op1=ALU.add))
                dve.sem_inc(s_gused, 1)

            def gate_logit_terms(b):
                dve.wait_ge(s_g2, 16)
                dve.wait_ge(s_grelu, b + 1)
                for d in range(KD):
                    last = dve.tensor_scalar(gp[:, d, :], g2s[:, d, :], gt[:, d:d + 1], None, ALU.mult)
                last.then_inc(s_gmix, 1)

            def gate_max(b):
                dve.wait_ge(s_gps, 2 * b + 2)
                link(dve.reduce_max(ginv[:, :], aps[1][:, 0:NETS], AX_X))
                dve.tensor_scalar(nmax[:, :], ginv[:, :], -1.0, None, ALU.mult).then_inc(s_gmax, 1)

            def gate_weights(b):
                dve.wait_ge(s_gexp, b + 1)
                link(dve.reciprocal(ginv[:, :], gsum[:, :]))
                link(dve.tensor_scalar(gw[:, :], gexp[:, :], ginv[:, 0:1], None, ALU.mult))

            def mix(s, k, step):
                net = [2, 0, 1][step]
                g = GATE_PART[net]
                base = 12 * (2 * s + k)
                if step == 0:
                    dve.wait_ge(s_xs, 2 * s + k + 1)
                    dve.wait_ge(s_yacc, KD * (4 * PAIRS * (s + 1) - 1 + k))
                for d in range(KD):
                    if step:
                        dve.wait_ge(s_mix, base + 4 * (step - 1) + d + 1)
                    dve.scalar_tensor_tensor(out=Y[:, 2, k, d, :], in0=Y[:, net, k, d, :], scalar=gw[:, g:g + 1],
                                             in1=Y[:, 2, k, d, :] if step else xaux[:, d, :],
                                             op0=ALU.mult, op1=ALU.add).then_inc(s_mix, 1)

            def x2_low(s, k):
                for d in range(KD):
                    dve.wait_ge(s_chi, KD * (2 * s + k) + d + 1)
                    dve.tensor_tensor(xl[:, s % 2, k, d, :], Y[:, 2, k, d, :],
                                      xh[:, s % 2, k, d, :].bitcast(F32), ALU.subtract).then_inc(s_clo, 1)

            def out_tiles(s, k, tiles):
                dve.wait_ge(s_bias, 16 * (s // 2 + 1))
                dve.wait_ge(s_mix, 12 * (2 * s + k) + 12)
                for t in tiles:
                    T = TT * (2 * s + k) + t
                    dve.wait_ge(s_ops, T + 1)
                    dve.tensor_tensor(Y[:, 1, k, t, :], aps[T % 2][:, :], bias_bc[:, :],
                                      ALU.add).then_inc(s_oev, 1)

            def steps(s, net, p, which):
                pair = s * PAIRS + p
                for v in range(UNITS):
                    final = which == "last" and s == SUPERS - 1
                    if not (final and v == UNITS - 1):
                        hidden_low(UNITS * pair + v + 1, v + 1)
                    if v == 0:
                        split_low(1, 2 * pair + 1)
                    if v == 4 and not final:
                        split_low(0, 2 * pair + 2)
                    if which == "last" and v == 7 and s % 2 == 0:
                        gate_max(s // 2)
                    if v % 2:
                        accumulate(s, 4 * pair + v // 2, net, (v // 2) % 2, which == "first" and v < 4)
                    if which == "first" and s > 0:
                        if v == 0:
                            mix(s - 1, 0, 0)
                            mix(s - 1, 0, 1)
                        if v == 1:
                            mix(s - 1, 0, 2)
                            x2_low(s - 1, 0)
                        if v == 2:
                            mix(s - 1, 1, 0)
                            mix(s - 1, 1, 1)
                            out_tiles(s - 1, 0, (0, 1))
                            mix(s - 1, 1, 2)
                            out_tiles(s - 1, 0, (2,))
                            x2_low(s - 1, 1)
                            out_tiles(s - 1, 0, (3,))
                        if v == 4:
                            out_tiles(s - 1, 1, range(TT))
                    if which == "last":
                        if v == 2 and s + 1 < SUPERS:
                            x_low(s + 1, 0)
                        if v == 5 and s % 2 == 0:
                            gate_partial(s // 2, 2)
                        if v == 6:
                            if s + 1 < SUPERS:
                                x_low(s + 1, 1)
                            if s % 2 == 0:
                                gate_logit_terms(s // 2)
                        if v == 7 and s % 2 == 0:
                            gate_weights(s // 2)

            x_low(0, 0)
            split_low(0, 0)
            hidden_low(0, 0)
            x_low(0, 1)
            for s in range(SUPERS):
                steps(s, 0, 0, "first")
                with dve.Fori(1, NET_PAIRS) as p:
                    steps(s, 0, p, "middle")
                if s % 2 == 0:
                    gate_partial(s // 2, 0)
                dve.wait_ge(s_zero, 2 + 4 * s)
                with dve.Fori(NET_PAIRS, 6) as p:
                    steps(s, 1, p, "middle")
                if s % 2 == 0:
                    dve.wait_ge(s_g, 16 * (4 * (s // 2) + 2))
                    dve.wait_ge(s_c, 2)
                    for d in range(KD):
                        diag = gaux[:, d, d * P:(d + 1) * P]
                        dve.tensor_tensor(diag, diag, ident[:, :], ALU.add).then_inc(s_Wi, 1)
                    for d in range(KD):
                        dve.wait_ge(s_Whi, KD * (s // 2) + d + 1)
                        last = dve.tensor_tensor(Wl[:, d, :], gaux[:, d, :], Wh[:, d, :].bitcast(F32),
                                                 ALU.subtract)
                        last.then_inc(s_Wrdy, 1)
                    dve.wait_ge(s_Wrdy, KD * (s // 2 + 1))
                    dve.sem_inc(s_gused, 1)
                with dve.Fori(6, 2 * NET_PAIRS) as p:
                    steps(s, 1, p, "middle")
                if s % 2 == 0:
                    gate_partial(s // 2, 1)
                with dve.Fori(2 * NET_PAIRS, PAIRS - 1) as p:
                    steps(s, 2, p, "middle")
                steps(s, 2, PAIRS - 1, "last")
            for k in range(2):
                for step in range(3):
                    mix(SUPERS - 1, k, step)
                x2_low(SUPERS - 1, k)
            for k in range(2):
                out_tiles(SUPERS - 1, k, range(TT))

        @block.tensor
        def _(pe):
            def product(dst, stationary, moving, start, stop):
                pairs = ((0, 0), (0, 1), (1, 0))
                for i, (a, b) in enumerate(pairs):
                    last = pe.matmul(dst, stationary[a], moving[b], start=start and i == 0, stop=stop and i == 2)
                return last

            def up(s, v, U):
                slot, k, c = v // 4, (v // 2) % 2, v % 2
                for d in range(KD):
                    cols = slice(d * GF + c * P, d * GF + (c + 1) * P)
                    last = product(hps[v % 2][:, :], (wh[:, slot, cols], wl[:, slot, cols]),
                                   (xh[:, s % 2, k, d, :], xl[:, s % 2, k, d, :]), d == 0, d == KD - 1)
                last.then_inc(s_hps, 1)

            def down(v, U, K):
                slot, c = v // 4, v % 2
                pe.wait_ge(s_hrdy, U + 1)
                for d in range(KD):
                    if c == 0 and not (isinstance(K, int) and K == 0):
                        pe.wait_ge(s_yacc, KD * K + d + 1 - KD)
                    c0 = KD * GF + c * D + d * P
                    last = product(yps[d][:, :], (wh[:, slot, c0:c0 + P], wl[:, slot, c0:c0 + P]),
                                   (hh[:, v % 2, :], hl[:, v % 2, :]), c == 0, c == GC - 1)
                    if c == GC - 1:
                        last.then_inc(s_yps, 1)

            def transpose_x(s, k, pieces):
                src = gaux if (s == 0 and k == 1) else xaux
                if 0 in pieces:
                    pe.wait_ge(s_x[k], 16 * (s + 1))
                    pe.wait_ge(s_c, 1)
                    if s > 1 and k == 0:
                        pe.wait_ge(s_oev, TT * 2 * (s - 1))
                for d in pieces:
                    X = 8 * s + 4 * k + d
                    if X >= 2:
                        pe.wait_ge(s_xlo, X - 1)
                    for t in range(TT):
                        last = pe.transpose(aps[X % 2][:, t * P:(t + 1) * P], src[:, t, d * P:(d + 1) * P],
                                            ident[:, :])
                    last.then_inc(s_xtr, 1)

            def gate_hidden(b):
                pe.wait_ge(s_gused, 4 * b + 4)
                pe.wait_ge(s_c, 2)
                pe.wait_ge(s_xlo, 8 * min(2 * b + 2, SUPERS))
                for d in range(KD):
                    last = pe.matmul(aps[0][:, d:d + 1], gacc[:, d * P:(d + 1) * P], ones[:, 0:1],
                                     start=True, stop=True)
                last.then_inc(s_gps, 1)

            def gate_logits(b):
                pe.wait_ge(s_gmix, b + 1)
                for d in range(KD):
                    last = pe.matmul(aps[1][:, 0:NETS], ones[:, :], gp[:, d, :], start=d == 0, stop=d == KD - 1)
                last.then_inc(s_gps, 1)

            def category(s, k):
                pe.wait_ge(s_clo, KD * (2 * s + k + 1))
                pe.wait_ge(s_Wrdy, KD * (s // 2 + 1))
                pe.wait_ge(s_xlo, 8 * min(s + 2, SUPERS))
                pe.wait_ge(s_gexp, s // 2 + 1)
                for t in range(TT):
                    T = TT * (2 * s + k) + t
                    if T >= 2:
                        pe.wait_ge(s_oev, T - 1)
                    tok = slice(t * P, (t + 1) * P)
                    for d in range(KD):
                        last = product(aps[T % 2][:, :], (xh[:, s % 2, k, d, tok], xl[:, s % 2, k, d, tok]),
                                       (Wh[:, d, :], Wl[:, d, :]), d == 0, d == KD - 1)
                    last.then_inc(s_ops, 1)

            def steps(s, p, which):
                pair = s * PAIRS + p
                for v in range(UNITS):
                    U = UNITS * pair + v
                    wrap = v == UNITS - 1
                    final = which == "last" and s == SUPERS - 1
                    prep = which == "last" and s + 1 < SUPERS and v in (2, 6)
                    if prep:
                        transpose_x(s + 1, v // 4, (0, 1))
                    if not (final and wrap):
                        if v % 4 == 3:
                            pe.wait_ge(s_wrdy, 2 * pair + (v + 1) // 4 + 1)
                        if which == "last" and wrap:
                            pe.wait_ge(s_xlo, 8 * (s + 1) + 4)
                        if which == "first" and v == 1:
                            pe.wait_ge(s_xlo, 8 * s + 8)
                        up(s + 1 if which == "last" and wrap else s, (v + 1) % UNITS, U + 1)
                    if prep:
                        transpose_x(s + 1, v // 4, (2, 3))
                    if which == "last" and wrap and s % 2 == 0:
                        gate_logits(s // 2)
                    down(v, U, 4 * pair + v // 2)
                    if which == "last" and v == 6 and s % 2 == 0:
                        gate_hidden(s // 2)
                    if which == "first" and s > 0:
                        if v == 2:
                            category(s - 1, 0)
                        if v == 4:
                            category(s - 1, 1)

            transpose_x(0, 0, (0, 1, 2, 3))
            pe.wait_ge(s_wrdy, 1)
            pe.wait_ge(s_xlo, 4)
            up(0, 0, 0)
            transpose_x(0, 1, (0, 1, 2, 3))
            for s in range(SUPERS):
                steps(s, 0, "first")
                with pe.Fori(1, PAIRS - 1) as p:
                    steps(s, p, "middle")
                steps(s, PAIRS - 1, "last")
            for k in range(2):
                category(SUPERS - 1, k)


_INS = ["x", "itok_B_0_2", "itok_B_0_63", "L0_cond_wi", "L0_cond_wo", "L0_cond_swi", "L0_cond_swo",
        "L0_cond_g1", "L0_cond_g2", "L1_cond_W", "L1_cond_b"]


def kernel(**inputs):
    import numpy as _np
    import concourse.bacc as _bacc
    from concourse import mybir as _mybir
    from concourse.bass_utils import run_bass_kernel_spmd as _run

    nc = _bacc.Bacc("TRN2", target_bir_lowering=False, num_devices=1)
    arrays, args = {}, []
    for name in _INS:
        a = _np.ascontiguousarray(inputs[name])
        arrays[f"in_{name}_dram"] = a
        args.append(nc.dram_tensor(f"in_{name}_dram", a.shape, _mybir.dt.from_np(a.dtype), kind="ExternalInput").ap())
    out = nc.dram_tensor("out_dram", inputs["x"].shape, _mybir.dt.float32, kind="ExternalOutput").ap()
    build(nc, *args, out)
    r = _run(nc, [arrays], core_ids=[0])
    return r.results[0]["out_dram"]
```

```python
from contextlib import ExitStack

import concourse.bass as bass
from concourse import mybir

F32 = mybir.dt.float32
F32R = mybir.dt.float32r
I32 = mybir.dt.int32
ALU = mybir.AluOpType
ACT = mybir.ActivationFunctionType
AX_X = mybir.AxisListType.X

P = 128
D = 512
F = 2048
KD = D // P
TB = 512
TT = TB // P
NBATCH, SEQ = 2, 2048
SUPERS = NBATCH * SEQ // (2 * TB)
NETS = 3
GF = 256
GC = GF // P
GROUPS = NETS * F // GF
PAIRS = GROUPS // 2
NET_PAIRS = PAIRS // NETS
WCOLS = KD * GF + GC * D
PIECE = 512
PIECES = WCOLS // PIECE
WARM_UP = 6
UNITS = 8
GATE_PART = [1, 2, 0]


def mixed(s):
    return NETS * KD * s


def mix_net(s):
    return 0 if s == SUPERS - 1 else 2


def build(nc, x, expert_id, category_id, wi, wo, swi, swo, g1, g2, W, bias, out):
    x_blk = x.rearrange("a (n p t) d -> (a n) p t d", p=P, t=TT)
    out_blk = out.rearrange("a (n p t) d -> (a n) p t d", p=P, t=TT)
    wi_v = wi.rearrange("e (k p) f -> e p k f", p=P)
    wo_v = wo.rearrange("e (c p) d -> e p c d", p=P)
    swi_v = swi.rearrange("e (k p) f -> e p k f", p=P)
    swo_v = swo.rearrange("e (c p) d -> e p c d", p=P)
    g1_v = g1.rearrange("(i k p) m -> i p k m", p=P, k=KD)
    g2_v = g2.rearrange("(k p) c -> p k c", p=P)
    W_v = W.rearrange("e (k p) h -> e p k h", p=P)

    ctx = ExitStack()
    with ctx:
        def sb(name, shape, dt=F32):
            return ctx.enter_context(nc.sbuf_tensor(name, shape, dt))

        def sem(name):
            return ctx.enter_context(nc.semaphore(name))

        xh = sb("xh", [P, 2, 2, KD, TB], F32R)
        xl = sb("xl", [P, 2, 2, KD, TB], F32R)
        Y = sb("Y", [P, NETS, 2, KD, TB])
        wh = sb("wh", [P, 2, WCOLS], F32R)
        wl = sb("wl", [P, 2, WCOLS], F32R)
        wraw = sb("wraw", [P, 2, WCOLS])
        hh = sb("hh", [P, 2, TB], F32R)
        hl = sb("hl", [P, 2, TB], F32R)
        Wh = sb("Wh", [P, KD, D], F32R)
        Wl = sb("Wl", [P, KD, D], F32R)
        xaux = sb("xaux", [P, KD, TB])
        gaux = sb("gaux", [P, KD, D])
        gacc = sb("gacc", [P, D])
        bias_bc = sb("bias_bc", [P, D])
        ident = sb("ident", [P, P])
        ones = sb("ones", [P, P])
        g2s = sb("g2s", [P, KD, NETS])
        gt = sb("gt", [P, KD])
        gp = sb("gp", [P, KD, NETS])
        nmax = sb("nmax", [P, 1])
        gexp = sb("gexp", [P, NETS])
        gsum = sb("gsum", [P, 1])
        ginv = sb("ginv", [P, 1])
        gw = sb("gw", [P, NETS])
        ids = sb("ids", [1, 4], I32)

        yps = [ctx.enter_context(nc.psum_tensor(f"yps{j}", [P, TB], F32)) for j in range(KD)]
        hps = [ctx.enter_context(nc.psum_tensor(f"hps{j}", [P, TB], F32)) for j in range(2)]
        aps = [ctx.enter_context(nc.psum_tensor(f"aps{j}", [P, TB], F32)) for j in range(2)]

        s_ids = sem("ids_loaded")
        s_x = [sem("x_loaded_even"), sem("x_loaded_odd")]
        s_x0 = [sem("first_tokens_loaded_0"), sem("first_tokens_loaded_1")]
        s_w0 = [sem("first_up_weights_loaded_0"), sem("first_up_weights_loaded_1")]
        s_w0rdy = sem("first_up_weights_ready")
        s_w = [sem("weights_loaded_0"), sem("weights_loaded_1")]
        s_g = sem("gaux_loaded")
        s_g2 = sem("g2_loaded")
        s_bias = sem("bias_loaded")
        s_stored = [sem("out_stored_block_0"), sem("out_stored_block_1")]
        s_c = sem("ident_set")
        s_ident = sem("ident_cleared")
        s_ones = sem("ones_set")
        s_xtr = sem("x_transposed")
        s_xhi = sem("x_high_split")
        s_xlo = sem("x_low_split")
        s_whi = sem("weights_high_split")
        s_wrdy = sem("weights_ready")
        s_hps = sem("hidden_in_psum")
        s_hhi = sem("hidden_high_split")
        s_hrdy = sem("hidden_ready")
        s_yps = sem("net_out_in_psum")
        s_yacc = sem("net_out_accumulated")
        s_zero = sem("net_out_cleared")
        s_gused = sem("gaux_used")
        s_gch = sem("gate_vector_step")
        s_gps = sem("gate_product_in_psum")
        s_grelu = sem("gate_hidden_ready")
        s_gexp = sem("gate_exp_ready")
        s_gmix = sem("gate_product_ready")
        s_gmax = sem("gate_max_ready")
        s_xs = sem("x_summed")
        s_mix = [sem("mix_step_block_0"), sem("mix_step_block_1")]
        s_chi = sem("x2_high_split")
        s_clo = sem("x2_low_split")
        s_Wi = sem("category_identity_added")
        s_Whi = sem("category_high_split")
        s_Wrdy = sem("category_ready")
        s_ops = sem("out_in_psum")
        s_oev = sem("out_evacuated")

        block = ctx.enter_context(nc.Block())

        @block.sync
        def _(sp):
            def load_weights(s, net, p, j, e):
                m = s * GROUPS + net * 2 * NET_PAIRS + 2 * p + j
                f0 = p * 2 * GF + j * GF
                c0 = p * 2 * GC + j * GC
                if not isinstance(m, int) or m >= 2:
                    sp.wait_ge(s_wrdy, m - 1)
                src_i, src_o, n = (swi_v, swo_v, net) if net < 2 else (wi_v, wo_v, e)
                sp.dma_start(wraw[:, j, 0:KD * GF].rearrange("p (k f) -> p k f", k=KD),
                             src_i[n, :, :, bass.ds(f0, GF)]).then_inc(s_w[j], 16)
                sp.dma_start(wraw[:, j, KD * GF:WCOLS].rearrange("p (c d) -> p c d", c=GC),
                             src_o[n, :, bass.ds(c0, GC), :]).then_inc(s_w[j], 16)

            for h in range(2):
                ks = slice(2 * h, 2 * h + 2)
                sp.dma_start(xaux[:, :, 2 * h * P:(2 * h + 2) * P],
                             x_blk[0, :, :, 2 * h * P:(2 * h + 2) * P]).then_inc(s_x0[h], 16)
                sp.dma_start(wraw[:, 0, 2 * h * GF:(2 * h + 2) * GF].rearrange("p (k f) -> p k f", k=2),
                             swi_v[0, :, ks, 0:GF]).then_inc(s_w0[h], 16)
            for c in range(GC):
                c0 = KD * GF + c * D
                sp.dma_start(wraw[:, 0, c0:c0 + D], swo_v[0, :, c, :]).then_inc(s_w[0], 16)
            sp.dma_start(gaux[:, :, :], x_blk[1, :, :, :]).then_inc(s_x[1], 16)
            load_weights(0, 0, 0, 1, None)
            sp.dma_start(ids[:, 0:2], expert_id.rearrange("(a n) -> a n", a=1)).then_inc(s_ids, 16)
            sp.dma_start(ids[:, 2:4], category_id.rearrange("(a n) -> a n", a=1)).then_inc(s_ids, 16)
            sp.dma_start(g2s[:, :, :], g2_v).then_inc(s_g2, 16)
            sp.wait_ge(s_ids, 32)
            experts = [sp.value_load(ids[0:1, b:b + 1], min_val=0, max_val=wi.shape[0] - 1) for b in range(NBATCH)]
            cats = [sp.value_load(ids[0:1, 2 + b:3 + b], min_val=0, max_val=W.shape[0] - 1) for b in range(NBATCH)]

            def store(t):
                sp.wait_ge(s_oev, TT * (t + 1))
                sp.dma_start(out_blk[t, :, :, :], Y[:, 1, t % 2, :, :]).then_inc(s_stored[t % 2], 16)

            for s in range(SUPERS):
                b, first_half = s // 2, s % 2 == 0
                e = experts[b]
                if s > 0:
                    load_weights(s, 0, 0, 0, e)
                    load_weights(s, 0, 0, 1, e)
                    sp.wait_ge(s_xtr, 8 * s + 4)
                    sp.dma_start(xaux[:, :, :], x_blk[2 * s + 1, :, :, :]).then_inc(s_x[1], 16)
                load_weights(s, 0, 1, 0, e)
                load_weights(s, 0, 1, 1, e)
                load_weights(s, 0, 2, 0, e)
                if s > 0:
                    store(2 * s - 2)
                load_weights(s, 0, 2, 1, e)
                if s > 0:
                    store(2 * s - 1)
                if first_half:
                    if s == 0:
                        sp.wait_ge(s_xtr, 8)
                    else:
                        sp.wait_ge(s_mix[1], mixed(s))
                    sp.dma_start(gaux[:, :, :], g1_v[GATE_PART[0], :, :, :]).then_inc(s_g, 16)
                    sp.dma_start(bias_bc[:, :], bias[bass.ds(cats[b], 1), :].to_broadcast([P, D])).then_inc(s_bias, 16)
                load_weights(s, 0, 3, 0, e)
                load_weights(s, 0, 3, 1, e)
                with sp.Fori(0, 2) as p:
                    for j in range(2):
                        load_weights(s, 1, p, j, e)
                if first_half:
                    sp.wait_ge(s_gused, 4 * b + 1)
                    sp.dma_start(gaux[:, :, :], W_v[cats[b], :, :, :]).then_inc(s_g, 16)
                if s + 1 < SUPERS:
                    if s > 0:
                        sp.wait_ge(s_mix[0], mixed(s))
                    else:
                        sp.wait_ge(s_xtr, 4)
                    sp.dma_start(xaux[:, :, :], x_blk[2 * s + 2, :, :, :]).then_inc(s_x[0], 16)
                with sp.Fori(2, 4) as p:
                    for j in range(2):
                        load_weights(s, 1, p, j, e)
                if first_half:
                    sp.wait_ge(s_gused, 4 * b + 2)
                    sp.dma_start(gaux[:, :, :], g1_v[GATE_PART[1], :, :, :]).then_inc(s_g, 16)
                with sp.Fori(0, 2) as p:
                    for j in range(2):
                        load_weights(s, 2, p, j, e)
                if first_half:
                    sp.wait_ge(s_gused, 4 * b + 3)
                    sp.dma_start(gaux[:, :, :], g1_v[GATE_PART[2], :, :, :]).then_inc(s_g, 16)
                with sp.Fori(2, 4) as p:
                    for j in range(2):
                        load_weights(s, 2, p, j, e)
            store(2 * SUPERS - 2)
            for t in range(TT):
                sp.wait_ge(s_oev, TT * (2 * SUPERS - 1) + t + 1)
                sp.dma_start(out_blk[2 * SUPERS - 1, :, t, :], Y[:, 1, 1, t, :]).then_inc(s_stored[1], 16)
            sp.wait_ge(s_stored[0], 16 * SUPERS)
            sp.wait_ge(s_stored[1], 16 * (SUPERS - 1 + TT))

        @block.gpsimd
        def _(pool):
            pool.memset(ones[:, :], 1.0).then_inc(s_ones, 1)
            pool.memset(ident[:, :], 0.0).then_inc(s_ident, 1)
            pool.wait_ge(s_ident, 1)
            pool.affine_select(out=ident[:, :], in_=ident[:, :], compare_op=ALU.not_equal, fill=1.0,
                               base=0, pattern=[[-1, P]], channel_multiplier=1).then_inc(s_c, 1)
            pool.memset(Y[:, 1, :, :, :], 0.0).then_inc(s_zero, 1)
            pool.memset(Y[:, 2, :, :, :], 0.0).then_inc(s_zero, 1)
            for s in range(SUPERS):
                q = s % 2
                pool.wait_ge(s_xlo, 8 * (s + 1))
                for k, into in enumerate((xaux, gaux)):
                    if k == 0:
                        pool.wait_ge(s_xtr, 8 * min(s + 2, SUPERS))
                    else:
                        pool.wait_ge(s_gused, 4 * (s // 2 + 1))
                    if s > 0:
                        pool.wait_ge(s_mix[k], mixed(s))
                    pool.tensor_tensor(into[:, :, :], xh[:, q, k, :, :].bitcast(F32),
                                       xl[:, q, k, :, :].bitcast(F32), ALU.add).then_inc(s_xs, 1)
                if s + 1 < SUPERS:
                    for k in range(2):
                        pool.wait_ge(s_clo, KD * (2 * s + k + 1))
                        pool.memset(Y[:, 2, k, :, :], 0.0).then_inc(s_zero, 1)
                    for k in range(2):
                        pool.wait_ge(s_stored[k], 16 * (s + 1))
                        pool.memset(Y[:, 1, k, :, :], 0.0).then_inc(s_zero, 1)

        @block.scalar
        def _(act):
            def hidden_high(U, i):
                act.wait_ge(s_hps, U + 1)
                act.activation(hh[:, i % 2, :], hps[i % 2][:, :], ACT.Relu).then_inc(s_hhi, 1)

            def split_high(pair, slot, pieces=range(PIECES)):
                act.wait_ge(s_w[slot], 32 * (pair + 1))
                for c in pieces:
                    cols = slice(c * PIECE, (c + 1) * PIECE)
                    act.activation(wh[:, slot, cols], wraw[:, slot, cols], ACT.Copy).then_inc(s_whi, 1)

            def x_high(s, k, pieces):
                for d in pieces:
                    X = 8 * s + 4 * k + d
                    act.wait_ge(s_xtr, X + 1)
                    act.activation(xh[:, s % 2, k, d, :], aps[X % 2][:, :], ACT.Copy).then_inc(s_xhi, 1)

            def x2_high(s, k):
                for d in range(KD):
                    if s < SUPERS - 1:
                        act.wait_ge(s_mix[k], mixed(s) + 8 + d + 1)
                    else:
                        act.wait_ge(s_yacc, KD * (4 * PAIRS * SUPERS - 2 + k) + d + 1)
                    act.activation(xh[:, s % 2, k, d, :], Y[:, mix_net(s), k, d, :], ACT.Copy).then_inc(s_chi, 1)

            def steps(s, p, which):
                pair = s * PAIRS + p
                for v in range(UNITS):
                    end = which == "last" and v == UNITS - 1 and s == SUPERS - 1
                    prep = which == "last" and s + 1 < SUPERS and v in (2, 6)
                    if prep:
                        x_high(s + 1, v // 4, (0, 1))
                    if not end:
                        hidden_high(UNITS * pair + v + 1, v + 1)
                    if which == "first" and s == 0 and v == 0:
                        x_high(0, 1, (2, 3))
                    if v == 0:
                        split_high(pair, 1)
                    if v == 4 and not (which == "last" and s == SUPERS - 1):
                        split_high(pair + 1, 0)
                    if which == "first" and s % 2 and v == 0:
                        act.wait_ge(s_gmax, s // 2 + 1)
                        act.activation(gexp[:, :], aps[1][:, 0:NETS], ACT.Exp, bias=nmax[:, 0:1],
                                       accum_out=gsum[:, 0:1]).then_inc(s_gexp, 1)
                    if which == "first" and s > 0:
                        if v in (3, 6):
                            x2_high(s - 1, (v - 3) // 3)
                    if prep:
                        x_high(s + 1, v // 4, (2, 3))
                    if which == "last":
                        if s == SUPERS - 1 and v in (5, 7):
                            x2_high(s, (v - 5) // 2)
                        if v == 7 and s % 2 == 0:
                            act.wait_ge(s_gps, s + 1)
                            act.activation(gt[:, :], aps[0][:, 0:KD], ACT.Relu).then_inc(s_grelu, 1)

            for h in range(2):
                x_high(0, 0, (2 * h, 2 * h + 1))
                act.wait_ge(s_w0[h], 16)
                cols = slice(h * PIECE, (h + 1) * PIECE)
                act.activation(wh[:, 0, cols], wraw[:, 0, cols], ACT.Copy).then_inc(s_whi, 1)
            split_high(0, 0, (2, 3))
            hidden_high(0, 0)
            x_high(0, 1, (0, 1))
            for s in range(SUPERS):
                steps(s, 0, "first")
                with act.Fori(1, 6) as p:
                    steps(s, p, "middle")
                if s % 2 == 0:
                    for d in range(KD):
                        act.wait_ge(s_Wi, 4 * (s // 2) + d + 1)
                        act.activation(Wh[:, d, :], gaux[:, d, :], ACT.Copy).then_inc(s_Whi, 1)
                with act.Fori(6, PAIRS - 1) as p:
                    steps(s, p, "middle")
                steps(s, PAIRS - 1, "last")

        @block.vector
        def _(dve):
            def hidden_low(U, i):
                dve.wait_ge(s_hhi, U + 1)
                dve.scalar_tensor_tensor(out=hl[:, i % 2, :], in0=hps[i % 2][:, :], scalar=0.0,
                                         in1=hh[:, i % 2, :].bitcast(F32), op0=ALU.max,
                                         op1=ALU.subtract).then_inc(s_hrdy, 1)

            def split_low(slot, m, pieces=range(PIECES)):
                for c in pieces:
                    cols = slice(c * PIECE, (c + 1) * PIECE)
                    dve.wait_ge(s_whi, PIECES * m + c + 1)
                    last = dve.tensor_tensor(wl[:, slot, cols], wraw[:, slot, cols],
                                             wh[:, slot, cols].bitcast(F32), ALU.subtract)
                last.then_inc(s_wrdy, 1)

            def accumulate(s, K, net, k, copy):
                for d in range(KD):
                    dve.wait_ge(s_yps, KD * K + d + 1)
                    if copy:
                        if s > 0:
                            dve.wait_ge(s_mix[k], mixed(s - 1) + KD)
                        dve.tensor_copy(Y[:, net, k, d, :], yps[d][:, :]).then_inc(s_yacc, 1)
                    else:
                        dve.wait_ge(s_yacc, KD * K + d + 1 - 2 * KD)
                        dve.tensor_tensor(Y[:, net, k, d, :], yps[d][:, :], Y[:, net, k, d, :],
                                          ALU.add).then_inc(s_yacc, 1)

            def x_low(s, k, pieces):
                for d in pieces:
                    X = 8 * s + 4 * k + d
                    dve.wait_ge(s_xhi, X + 1)
                    dve.tensor_tensor(xl[:, s % 2, k, d, :], aps[X % 2][:, :],
                                      xh[:, s % 2, k, d, :].bitcast(F32), ALU.subtract).then_inc(s_xlo, 1)

            chain = [0]

            def link(ins):
                chain[0] += 1
                ins.then_inc(s_gch, 1)
                dve.wait_ge(s_gch, chain[0])

            def gate_partial(b, net):
                n = [0, 2, 3][net]
                dve.wait_ge(s_g, 16 * (4 * b + n + 1))
                K = 4 * ((2 * b) * PAIRS + (net + 1) * NET_PAIRS) - 2
                dve.wait_ge(s_yacc, KD * (K + 1))
                for d in range(KD):
                    scalar = Y[:, net, 0, d, 0:1]
                    if net == 0 and d == 0:
                        link(dve.tensor_scalar(gacc[:, :], gaux[:, d, :], scalar, None, ALU.mult))
                    else:
                        link(dve.scalar_tensor_tensor(out=gacc[:, :], in0=gaux[:, d, :], scalar=scalar,
                                                      in1=gacc[:, :], op0=ALU.mult, op1=ALU.add))
                dve.sem_inc(s_gused, 1)

            def gate_logit_terms(b):
                dve.wait_ge(s_g2, 16)
                dve.wait_ge(s_grelu, b + 1)
                for d in range(KD):
                    last = dve.tensor_scalar(gp[:, d, :], g2s[:, d, :], gt[:, d:d + 1], None, ALU.mult)
                last.then_inc(s_gmix, 1)

            def gate_max(b):
                dve.wait_ge(s_gps, 2 * b + 2)
                link(dve.reduce_max(ginv[:, :], aps[1][:, 0:NETS], AX_X))
                dve.tensor_scalar(nmax[:, :], ginv[:, :], -1.0, None, ALU.mult).then_inc(s_gmax, 1)

            def gate_weights(b):
                dve.wait_ge(s_gexp, b + 1)
                link(dve.reciprocal(ginv[:, :], gsum[:, :]))
                link(dve.tensor_scalar(gw[:, :], gexp[:, :], ginv[:, 0:1], None, ALU.mult))

            def mix(s, k, net):
                last_super = s == SUPERS - 1
                held = (xaux, gaux)[k]
                g = GATE_PART[net]
                if net == 0:
                    dve.wait_ge(s_xs, 2 * s + k + 1)
                if net == 2:
                    dve.wait_ge(s_yacc, KD * (4 * PAIRS * (s + 1) - 1 + k - (2 if last_super else 0)))
                for d in range(KD):
                    if net:
                        dve.wait_ge(s_mix[k], mixed(s) + KD * (net - 1) + d + 1)
                    if last_super:
                        src, dst = Y[:, 0, k, d, :] if net else held[:, d, :], Y[:, 0, k, d, :]
                    else:
                        src, dst = held[:, d, :], Y[:, 2, k, d, :] if net == 2 else held[:, d, :]
                    dve.scalar_tensor_tensor(out=dst, in0=Y[:, net, k, d, :], scalar=gw[:, g:g + 1], in1=src,
                                             op0=ALU.mult, op1=ALU.add).then_inc(s_mix[k], 1)

            def mix_last(k):
                K = 4 * PAIRS * SUPERS - 2 + k
                g = GATE_PART[2]
                for d in range(KD):
                    dve.wait_ge(s_yps, KD * K + d + 1)
                    dve.wait_ge(s_mix[k], mixed(SUPERS - 1) + 8 + d + 1)
                    dve.scalar_tensor_tensor(out=Y[:, 0, k, d, :], in0=yps[d][:, :], scalar=gw[:, g:g + 1],
                                             in1=Y[:, 0, k, d, :], op0=ALU.mult, op1=ALU.add).then_inc(s_yacc, 1)

            def x2_low(s, k):
                for d in range(KD):
                    dve.wait_ge(s_chi, KD * (2 * s + k) + d + 1)
                    dve.tensor_tensor(xl[:, s % 2, k, d, :], Y[:, mix_net(s), k, d, :],
                                      xh[:, s % 2, k, d, :].bitcast(F32), ALU.subtract).then_inc(s_clo, 1)

            def out_tiles(s, k, tiles):
                dve.wait_ge(s_bias, 16 * (s // 2 + 1))
                dve.wait_ge(s_mix[k], mixed(s) + 12)
                for t in tiles:
                    T = TT * (2 * s + k) + t
                    dve.wait_ge(s_ops, T + 1)
                    dve.tensor_tensor(Y[:, 1, k, t, :], aps[T % 2][:, :], bias_bc[:, :],
                                      ALU.add).then_inc(s_oev, 1)

            def steps(s, net, p, which):
                pair = s * PAIRS + p
                for v in range(UNITS):
                    final = which == "last" and s == SUPERS - 1
                    prep = which == "last" and s + 1 < SUPERS and v in (2, 6)
                    if prep:
                        x_low(s + 1, v // 4, (0, 1))
                    if not (final and v == UNITS - 1):
                        hidden_low(UNITS * pair + v + 1, v + 1)
                    if which == "first" and s == 0 and v == 0:
                        x_low(0, 1, (2, 3))
                    if v == 0:
                        split_low(1, 2 * pair + 1)
                    if v == 4 and not final:
                        split_low(0, 2 * pair + 2)
                    if which == "last" and v == 7 and s % 2 == 0:
                        gate_logit_terms(s // 2)
                    if which == "first" and v == 0 and s % 2:
                        gate_max(s // 2)
                        gate_weights(s // 2)
                    if final and v > 4 and v % 2:
                        mix_last(v // 2 % 2)
                        x2_low(s, v // 2 % 2)
                    elif v % 2:
                        accumulate(s, 4 * pair + v // 2, net, (v // 2) % 2, which == "first" and v < 4)
                    if which == "first" and s > 0:
                        if v == 0:
                            mix(s - 1, 0, 0)
                        if v == 1:
                            mix(s - 1, 1, 0)
                        if v == 2:
                            mix(s - 1, 0, 1)
                            mix(s - 1, 0, 2)
                        if v == 3:
                            x2_low(s - 1, 0)
                        if v == 4:
                            mix(s - 1, 1, 1)
                        if v == 5:
                            out_tiles(s - 1, 0, (0, 1))
                            mix(s - 1, 1, 2)
                            out_tiles(s - 1, 0, (2, 3))
                        if v == 6:
                            x2_low(s - 1, 1)
                        if v == 7:
                            out_tiles(s - 1, 1, range(TT))
                    if prep:
                        x_low(s + 1, v // 4, (2, 3))
                    if final:
                        if v < 2:
                            mix(s, 0, v)
                        if v == 2:
                            mix(s, 0, 2)
                            mix(s, 1, 0)
                        if v in (3, 4):
                            mix(s, 1, v - 2)
                    if which == "last":
                        if v == 5 and s % 2 == 0:
                            gate_partial(s // 2, 2)

            for h in range(2):
                x_low(0, 0, (2 * h, 2 * h + 1))
                dve.wait_ge(s_whi, h + 1)
                cols = slice(h * PIECE, (h + 1) * PIECE)
                dve.tensor_tensor(wl[:, 0, cols], wraw[:, 0, cols], wh[:, 0, cols].bitcast(F32),
                                  ALU.subtract).then_inc(s_w0rdy, 1)
            split_low(0, 0, (2, 3))
            hidden_low(0, 0)
            x_low(0, 1, (0, 1))
            for s in range(SUPERS):
                steps(s, 0, 0, "first")
                with dve.Fori(1, NET_PAIRS) as p:
                    steps(s, 0, p, "middle")
                if s % 2 == 0:
                    gate_partial(s // 2, 0)
                dve.wait_ge(s_zero, 2 + 4 * s)
                with dve.Fori(NET_PAIRS, 6) as p:
                    steps(s, 1, p, "middle")
                if s % 2 == 0:
                    dve.wait_ge(s_g, 16 * (4 * (s // 2) + 2))
                    dve.wait_ge(s_c, 1)
                    for d in range(KD):
                        diag = gaux[:, d, d * P:(d + 1) * P]
                        dve.tensor_tensor(diag, diag, ident[:, :], ALU.add).then_inc(s_Wi, 1)
                    for d in range(KD):
                        dve.wait_ge(s_Whi, KD * (s // 2) + d + 1)
                        last = dve.tensor_tensor(Wl[:, d, :], gaux[:, d, :], Wh[:, d, :].bitcast(F32),
                                                 ALU.subtract)
                        last.then_inc(s_Wrdy, 1)
                    dve.wait_ge(s_Wrdy, KD * (s // 2 + 1))
                    dve.sem_inc(s_gused, 1)
                with dve.Fori(6, 2 * NET_PAIRS) as p:
                    steps(s, 1, p, "middle")
                if s % 2 == 0:
                    gate_partial(s // 2, 1)
                with dve.Fori(2 * NET_PAIRS, PAIRS - 1) as p:
                    steps(s, 2, p, "middle")
                steps(s, 2, PAIRS - 1, "last")
            for k in range(2):
                out_tiles(SUPERS - 1, k, range(TT))

        @block.tensor
        def _(pe):
            def product(dst, stationary, moving, start, stop):
                pairs = ((0, 0), (0, 1), (1, 0))
                for i, (a, b) in enumerate(pairs):
                    last = pe.matmul(dst, stationary[a], moving[b], start=start and i == 0, stop=stop and i == 2)
                return last

            def up(s, v, chunks=range(KD)):
                slot, k, c = v // 4, (v // 2) % 2, v % 2
                for d in chunks:
                    cols = slice(d * GF + c * P, d * GF + (c + 1) * P)
                    last = product(hps[v % 2][:, :], (wh[:, slot, cols], wl[:, slot, cols]),
                                   (xh[:, s % 2, k, d, :], xl[:, s % 2, k, d, :]), d == 0, d == KD - 1)
                if d == KD - 1:
                    last.then_inc(s_hps, 1)

            def down(v, U, K):
                slot, c = v // 4, v % 2
                pe.wait_ge(s_hrdy, U + 1)
                for d in range(KD):
                    if c == 0 and not (isinstance(K, int) and K == 0):
                        pe.wait_ge(s_yacc, KD * K + d + 1 - KD)
                    c0 = KD * GF + c * D + d * P
                    last = product(yps[d][:, :], (wh[:, slot, c0:c0 + P], wl[:, slot, c0:c0 + P]),
                                   (hh[:, v % 2, :], hl[:, v % 2, :]), c == 0, c == GC - 1)
                    if c == GC - 1:
                        last.then_inc(s_yps, 1)

            def transpose_x(s, k, pieces):
                src = gaux if (s == 0 and k == 1) else xaux
                if s == 0 and k == 0:
                    pe.wait_ge(s_x0[pieces[0] // 2], 16)
                elif 0 in pieces:
                    pe.wait_ge(s_x[k], 16 * (s + k))
                if 0 in pieces:
                    pe.wait_ge(s_c, 1)
                    if s > 1 and k == 0:
                        pe.wait_ge(s_oev, TT * 2 * (s - 1))
                for d in pieces:
                    X = 8 * s + 4 * k + d
                    if X >= 2:
                        pe.wait_ge(s_xlo, X - 1)
                    for t in range(TT):
                        last = pe.transpose(aps[X % 2][:, t * P:(t + 1) * P], src[:, t, d * P:(d + 1) * P],
                                            ident[:, :])
                    last.then_inc(s_xtr, 1)

            def gate_hidden(b):
                pe.wait_ge(s_gused, 4 * b + 4)
                pe.wait_ge(s_ones, 1)
                pe.wait_ge(s_xlo, 8 * min(2 * b + 2, SUPERS))
                for d in range(KD):
                    last = pe.matmul(aps[0][:, d:d + 1], gacc[:, d * P:(d + 1) * P], ones[:, 0:1],
                                     start=True, stop=True)
                last.then_inc(s_gps, 1)

            def gate_logits(b):
                pe.wait_ge(s_gmix, b + 1)
                for d in range(KD):
                    last = pe.matmul(aps[1][:, 0:NETS], ones[:, :], gp[:, d, :], start=d == 0, stop=d == KD - 1)
                last.then_inc(s_gps, 1)

            def category(s, k):
                pe.wait_ge(s_clo, KD * (2 * s + k + 1))
                pe.wait_ge(s_Wrdy, KD * (s // 2 + 1))
                pe.wait_ge(s_xlo, 8 * min(s + 2, SUPERS))
                pe.wait_ge(s_gexp, s // 2 + 1)
                for t in range(TT):
                    T = TT * (2 * s + k) + t
                    if T >= 2:
                        pe.wait_ge(s_oev, T - 1)
                    tok = slice(t * P, (t + 1) * P)
                    for d in range(KD):
                        last = product(aps[T % 2][:, :], (xh[:, s % 2, k, d, tok], xl[:, s % 2, k, d, tok]),
                                       (Wh[:, d, :], Wl[:, d, :]), d == 0, d == KD - 1)
                    last.then_inc(s_ops, 1)

            def steps(s, p, which):
                pair = s * PAIRS + p
                for v in range(UNITS):
                    U = UNITS * pair + v
                    wrap = v == UNITS - 1
                    final = which == "last" and s == SUPERS - 1
                    prep = which == "last" and s + 1 < SUPERS and v in (2, 6)
                    if prep:
                        transpose_x(s + 1, v // 4, (0, 1))
                    if not (final and wrap):
                        if v % 4 == 3:
                            pe.wait_ge(s_wrdy, 2 * pair + (v + 1) // 4 + 1)
                        if which == "last" and wrap:
                            pe.wait_ge(s_xlo, 8 * (s + 1) + 4)
                        if which == "first" and v == 1:
                            pe.wait_ge(s_xlo, 8 * s + 8)
                        up(s + 1 if which == "last" and wrap else s, (v + 1) % UNITS)
                    if which == "first" and s == 0 and v == 0:
                        transpose_x(0, 1, (2, 3))
                    if prep and v == 2:
                        transpose_x(s + 1, 0, (2, 3))
                    if which == "last" and wrap and s % 2 == 0:
                        gate_hidden(s // 2)
                    down(v, U, 4 * pair + v // 2)
                    if prep and v == 6:
                        transpose_x(s + 1, 1, (2, 3))
                    if which == "last" and wrap and s % 2 == 0:
                        gate_logits(s // 2)
                    if which == "first" and s > 0:
                        if v in (5, 7):
                            category(s - 1, (v - 5) // 2)

            pe.wait_ge(s_ones, 1)
            for _ in range(WARM_UP):
                pe.matmul(hps[1][:, 0:P], ones[:, :], ones[:, :], start=True, stop=True)
            for h in range(2):
                transpose_x(0, 0, (2 * h, 2 * h + 1))
            for h in range(2):
                pe.wait_ge(s_w0rdy, h + 1)
                pe.wait_ge(s_xlo, 2 * h + 2)
                up(0, 0, (2 * h, 2 * h + 1))
            pe.wait_ge(s_wrdy, 1)
            transpose_x(0, 1, (0, 1))
            for s in range(SUPERS):
                steps(s, 0, "first")
                with pe.Fori(1, PAIRS - 1) as p:
                    steps(s, p, "middle")
                steps(s, PAIRS - 1, "last")
            for k in range(2):
                category(SUPERS - 1, k)


_INS = ["x", "itok_B_0_2", "itok_B_0_63", "L0_cond_wi", "L0_cond_wo", "L0_cond_swi", "L0_cond_swo",
        "L0_cond_g1", "L0_cond_g2", "L1_cond_W", "L1_cond_b"]


def kernel(**inputs):
    import numpy as _np
    import concourse.bacc as _bacc
    from concourse import mybir as _mybir
    from concourse.bass_utils import run_bass_kernel_spmd as _run

    nc = _bacc.Bacc("TRN2", target_bir_lowering=False, num_devices=1)
    arrays, args = {}, []
    for name in _INS:
        a = _np.ascontiguousarray(inputs[name])
        arrays[f"in_{name}_dram"] = a
        args.append(nc.dram_tensor(f"in_{name}_dram", a.shape, _mybir.dt.from_np(a.dtype), kind="ExternalInput").ap())
    out = nc.dram_tensor("out_dram", inputs["x"].shape, _mybir.dt.float32, kind="ExternalOutput").ap()
    build(nc, *args, out)
    r = _run(nc, [arrays], core_ids=[0])
    return r.results[0]["out_dram"]
```
